# Optimizing a Trainium2 kernel written in Bass

```python
import numpy as np
import jax
import jax.numpy as jnp

def _softmax(x, axis=-1):
    return jax.nn.softmax(x, axis=axis)

def _gelu(x):
    return jax.nn.gelu(x, approximate=True)

def _silu(x):
    return jax.nn.silu(x)

def _sigmoid(x):
    return jax.nn.sigmoid(x)

def _layernorm(x, axis=-1, eps=1e-05):
    m = jnp.mean(x, axis=axis, keepdims=True)
    v = jnp.var(x, axis=axis, keepdims=True)
    return (x - m) / jnp.sqrt(v + eps)

def _scatter_add(tgt, idx, src, axis=0):
    return tgt.at[idx].add(src)

def _segment_sum(src, seg, n):
    return jax.ops.segment_sum(src, seg, n)
kernel_name = 'mk_xattn_seq_d1_seqx_r4_38ceb5'

def setup_inputs(seed: int=0):
    np.random.seed(seed)
    _w = jnp.asarray

    def _rec_inputs():
        import jax
        import jax.numpy as jnp
        _rk = jax.random.key(seed)
        x = -0.000125 + 0.9999 * jax.random.normal(jax.random.fold_in(_rk, 1), (32, 128, 512), jnp.float32)
        _lenS = 128 - jax.random.randint(jax.random.fold_in(_rk, 7), (32,), 0, max(1, 128 // 4) + 1, jnp.int32)
        _lenS2 = 128 - jax.random.randint(jax.random.fold_in(_rk, 8), (32,), 0, max(1, 128 // 4) + 1, jnp.int32)
        _ctx_1024P = jax.random.normal(jax.random.fold_in(_rk, 11), (32, 16, 256), jnp.float32)
        _ctx_1024c = jax.random.dirichlet(jax.random.fold_in(_rk, 511), 0.3 * jnp.ones((16,), jnp.float32), (32, 128))
        _ctx_1024t = jnp.einsum('bsk,bkd->bsd', _ctx_1024c, _ctx_1024P)
        _ctx_1024t = _ctx_1024t * jax.lax.rsqrt(jnp.mean(jnp.square(_ctx_1024t)) + 1e-12) * 0.953939
        ctx_1024 = 4.13588e-05 + 0.999923 * (_ctx_1024t + 0.3 * jax.random.normal(jax.random.fold_in(_rk, 611), (32, 128, 256), jnp.float32))
        return (x, ctx_1024)
    x, ctx_1024 = _rec_inputs()

    def _L0_xattn_setup():
        import jax, jax.numpy as jnp
        import numpy as np
        EPS = 1e-06

        def _rmsnorm(x, w):
            var = jnp.mean(jnp.square(x), axis=-1, keepdims=True)
            return x * jax.lax.rsqrt(var + EPS) * w
        key = jax.random.key(seed)
        ks = jax.random.split(key, 6)
        B, N, M = (4, 1024, 512)
        d_model, memory_dim = (512, 256)
        hidden_states = jax.random.normal(ks[0], (B, N, d_model), dtype=jnp.float32)
        memory = jax.random.normal(ks[1], (B, M, memory_dim), dtype=jnp.float32)
        W_mem = jax.random.normal(ks[2], (d_model, memory_dim), dtype=jnp.float32) / np.sqrt(memory_dim)
        W_gate = jax.random.normal(ks[3], (d_model, 2 * d_model), dtype=jnp.float32) / np.sqrt(2 * d_model)
        b_gate = jax.random.normal(ks[4], (d_model,), dtype=jnp.float32) * 0.01
        norm_w = jnp.ones((d_model,), dtype=jnp.float32)
        return {'hidden_states': hidden_states, 'memory': memory, 'W_mem': W_mem, 'W_gate': W_gate, 'b_gate': b_gate, 'norm_w': norm_w}
    _L0_xattn_all = _L0_xattn_setup()
    _L0_xattn_in = {k: v for k, v in _L0_xattn_all.items() if k in ('W_mem', 'W_gate', 'b_gate', 'norm_w')}
    del _L0_xattn_all
    return {'x': x, 'ctx_1024': ctx_1024, 'L0_xattn_W_mem': _L0_xattn_in['W_mem'], 'L0_xattn_W_gate': _L0_xattn_in['W_gate'], 'L0_xattn_b_gate': _L0_xattn_in['b_gate'], 'L0_xattn_norm_w': _L0_xattn_in['norm_w']}

def reference(x, ctx_1024, L0_xattn_W_mem, L0_xattn_W_gate, L0_xattn_b_gate, L0_xattn_norm_w):
    import jax
    import jax.numpy as jnp

    def _L0_xattn_ref(hidden_states, memory, W_mem, W_gate, b_gate, norm_w):
        import jax, jax.numpy as jnp
        import numpy as np
        EPS = 1e-06

        def _rmsnorm(x, w):
            var = jnp.mean(jnp.square(x), axis=-1, keepdims=True)
            return x * jax.lax.rsqrt(var + EPS) * w
        D = hidden_states.shape[-1]
        memory_proj = jnp.einsum('bme,de->bmd', memory, W_mem)
        scores = jnp.einsum('bnd,bmd->bnm', hidden_states, memory_proj) / jnp.sqrt(jnp.float32(D))
        attn = jax.nn.softmax(scores, axis=-1)
        memory_context = jnp.einsum('bnm,bmd->bnd', attn, memory_proj)
        gate_input = jnp.concatenate([hidden_states, memory_context], axis=-1)
        gate = jax.nn.sigmoid(jnp.einsum('bnf,df->bnd', gate_input, W_gate) + b_gate)
        fused = hidden_states + gate * memory_context
        return _rmsnorm(fused, norm_w)
    x = _L0_xattn_ref(x, ctx_1024, L0_xattn_W_mem, L0_xattn_W_gate, L0_xattn_b_gate, L0_xattn_norm_w)
    return x

_drawn_inputs = setup_inputs


def setup_inputs(seed=0):
    import zlib

    import numpy as np

    out = dict(_drawn_inputs(seed))
    spreads = {'L0_xattn_norm_w': (1.0, 0.2)}
    factors = {'L0_xattn_b_gate': 49.854}
    for name, (base, spread) in spreads.items():
        noise = np.random.default_rng([zlib.crc32(name.encode()), seed]).standard_normal(out[name].shape)
        drawn = base * np.exp(spread * noise) if base else spread * noise
        out[name] = jnp.asarray(drawn.astype(out[name].dtype))
    for name, factor in factors.items():
        out[name] = (out[name] * factor).astype(out[name].dtype)
    return out
```

```python
import concourse.bass as bass
from concourse import mybir
from contextlib import ExitStack

F32 = mybir.dt.float32
F32R = mybir.dt.float32r
BF16 = mybir.dt.bfloat16
ALU = mybir.AluOpType
ACT = mybir.ActivationFunctionType
AX = mybir.AxisListType

P = 128
B, S, D = 32, 128, 512
M, E = 128, 256
GB = 4
NG = B // GB
DC, EC = D // P, E // P
HALVES = (slice(0, D // 2), slice(D // 2, D))
SCALE = float(D) ** -0.5
EPS = 1e-6
WARM_UP = 12


def gated_cross_attention(nc, x, x_t, mem, mem_t, w_mem, w_mem_t, w_gate_t, b_gate, norm_w, out):
    ctx = ExitStack()
    with ctx:
        def sb(name, shape, dt=F32):
            return ctx.enter_context(nc.sbuf_tensor(name, shape, dt))

        def bank(name):
            return ctx.enter_context(nc.psum_tensor(name, [P, 512], F32))

        def sem(name):
            return ctx.enter_context(nc.semaphore(name))

        w_hi, w_lo = sb("w_hi", [P, DC, E], F32R), sb("w_lo", [P, DC, E], F32R)
        wt_hi, wt_lo = sb("wt_hi", [P, EC, D], F32R), sb("wt_lo", [P, EC, D], F32R)
        wx_hi, wx_lo = sb("wx_hi", [P, DC, D], F32R), sb("wx_lo", [P, DC, D], F32R)
        wc_hi, wc_lo = sb("wc_hi", [P, DC, D], F32R), sb("wc_lo", [P, DC, D], F32R)
        wa_hi, wa_lo = sb("wa_hi", [P, EC, D], F32R), sb("wa_lo", [P, EC, D], F32R)
        wt_raw = sb("wt_raw", [P, EC, D])
        wx_raw = sb("wx_raw", [P, DC, D])
        bias = sb("bias", [P, D])
        gain = sb("gain", [P, D])
        ident = sb("ident", [P, P])
        warm = sb("warm", [P, 512], BF16)

        xt_raw = sb("xt_raw", [P, 2, GB, DC, S])
        xt_hi, xt_lo = sb("xt_hi", [P, 2, GB, DC, S], F32R), sb("xt_lo", [P, 2, GB, DC, S], F32R)
        x_rows = sb("x_rows", [P, 2, GB, D])
        mt_raw = sb("mt_raw", [P, GB, EC, M])
        mt = sb("mt", [P, GB, EC, 2, M], F32R)
        m_raw = sb("m_raw", [P, GB, E])
        m_hi, m_lo = sb("m_hi", [P, GB, E], F32R), sb("m_lo", [P, GB, E], F32R)

        q_hi, q_lo = sb("q_hi", [P, EC, GB, S], F32R), sb("q_lo", [P, EC, GB, S], F32R)
        scores = sb("scores", [P, GB, M])
        row_max = sb("row_max", [P, GB])
        neg_bias = sb("neg_bias", [P, GB])
        exps = sb("exps", [P, GB, M])
        exp_sum = sb("exp_sum", [P, GB])
        inv_sum = sb("inv_sum", [P, GB])
        attn = sb("attn", [P, GB, M])
        at = sb("at", [P, GB, 2, S], F32R)
        a_sum = sb("a_sum", [P, GB, EC, S])
        a_hi, a_lo = sb("a_hi", [P, GB, EC, S], F32R), sb("a_lo", [P, GB, EC, S], F32R)

        row = sb("row", [P, 2, D])
        squares = sb("squares", [P, 2, D], BF16)
        mean_sq = sb("mean_sq", [P, GB])
        safe_sq = sb("safe_sq", [P, GB])
        eps, power = sb("eps", [P, 1]), sb("power", [P, 1])
        inv_rms = sb("inv_rms", [P, GB])
        result = sb("result", [P, GB, D])

        w_raw = row[:, :, :].rearrange("p a n -> p (a n)").rearrange("p (c e) -> p c e", c=DC)
        wc_raw = result[:, :, :]

        ps = [bank(f"ps{i}") for i in range(4)]
        ps_q, ps_s, ps_t, ps_a = ps[0:2], ps[2:4], ps[0], ps
        ps_gate = [bank("ps_gate0"), bank("ps_gate1")]
        ps_ctx = [bank("ps_ctx0"), bank("ps_ctx1")]

        ld_first = [sem(f"ld_first{c}") for c in range(DC)]
        ld_wc = [sem(f"ld_wc{c}") for c in range(DC)]
        ld_wx = [sem(f"ld_wx{c}") for c in range(DC)]
        ld_wt = sem("ld_wt")
        ld_bias, ld_gain = sem("ld_bias"), sem("ld_gain")
        ld_xt = [sem("ld_xt0"), sem("ld_xt1")]
        ld_rows = [sem("ld_rows0"), sem("ld_rows1")]
        ld_mt, ld_m = sem("ld_mt"), sem("ld_m")
        stored = [sem(f"stored{b}") for b in range(GB)]
        w_hi_done, w_lo_done = sem("w_hi_done"), sem("w_lo_done")
        wc_hi_done, wc_lo_done = sem("wc_hi_done"), sem("wc_lo_done")
        wx_hi_done, wx_lo_done = sem("wx_hi_done"), sem("wx_lo_done")
        wa_hi_done, wa_lo_done = sem("wa_hi_done"), sem("wa_lo_done")
        wt_hi_done, wt_lo_done = sem("wt_hi_done"), sem("wt_lo_done")
        xt_hi_done, xt_lo_done = sem("xt_hi_done"), sem("xt_lo_done")
        xt1_hi_done, xt1_lo_done = sem("xt1_hi_done"), sem("xt1_lo_done")
        mt_hi_done, mt_lo_done = sem("mt_hi_done"), sem("mt_lo_done")
        m_hi_done, m_lo_done = sem("m_hi_done"), sem("m_lo_done")
        m0_lo_done = sem("m0_lo_done")
        q_hi_done, q_lo_done = sem("q_hi_done"), sem("q_lo_done")
        at_hi_done, at_lo_done = sem("at_hi_done"), sem("at_lo_done")
        a_hi_done, a_lo_done = sem("a_hi_done"), sem("a_lo_done")
        s_sum_done, a_sum_done = sem("s_sum_done"), sem("a_sum_done")
        wa_made = sem("wa_made")
        q_made, s_made, t_made, a_made = sem("q_made"), sem("s_made"), sem("t_made"), sem("a_made")
        gate_made, ctx_made = sem("gate_made"), sem("ctx_made")
        max_done, bias_done, exp_done = sem("max_done"), sem("bias_done"), sem("exp_done")
        inv_done, attn_done = sem("inv_done"), sem("attn_done")
        z_done, tanh_done, u_done, fused_done = sem("z_done"), sem("tanh_done"), sem("u_done"), sem("fused_done")
        sq_done, safe_done = sem("sq_done"), sem("safe_done")
        rms_done, out_done = sem("rms_done"), sem("out_done")
        zeroed, constants, warm_ready = sem("zeroed"), sem("constants"), sem("warm_ready")

        block = ctx.enter_context(nc.Block())

        @block.sync
        def _(sp):
            def load_xt(g, p):
                sp.dma_start(xt_raw[:, p], x_t[g]).then_inc(ld_xt[p], 16)

            def load_rows(g, p):
                sp.dma_start(x_rows[:, p], x[g]).then_inc(ld_rows[p], 16)

            def load_mt(g):
                sp.dma_start(mt_raw[:, :, :, :], mem_t[g]).then_inc(ld_mt, 16)

            def load_m(g):
                sp.dma_start(m_raw[:, :, :], mem[g]).then_inc(ld_m, 16)

            def store(g, b):
                sp.wait_ge(out_done, GB * g + b + 1)
                sp.dma_start(out[g][:, b, :], result[:, b, :]).then_inc(stored[b], 16)

            def slots(g, p, first=False, left=NG):
                if not first:
                    store(g - 1, GB - 2)
                    store(g - 1, GB - 1)
                    if left > 1:
                        load_rows(g + 1, 1 - p)
                if left > 3:
                    if first:
                        sp.wait_ge(xt1_lo_done, GB)
                    else:
                        sp.wait_ge(xt_lo_done, GB * (g + 1))
                    load_xt(g + 3, 1 - p)
                if left > 2:
                    sp.wait_ge(mt_lo_done, g + 2)
                    load_mt(g + 2)
                store(g, 0)
                if left > 2:
                    sp.wait_ge(m_lo_done, g + 1)
                    load_m(g + 2)
                store(g, 1)

            for c in range(DC):
                sp.dma_start(w_raw[:, c, :], w_mem[:, c, :]).then_inc(ld_first[c], 16)
                sp.dma_start(xt_raw[:, 0, :, c, :], x_t[0][:, :, c, :]).then_inc(ld_first[c], 16)
            load_mt(0)
            for c in range(DC):
                sp.dma_start(wc_raw[:, c, :], w_gate_t[:, DC + c, :]).then_inc(ld_wc[c], 16)
            load_m(0)
            for c in range(DC):
                sp.dma_start(wx_raw[:, c, :], w_gate_t[:, c, :]).then_inc(ld_wx[c], 16)
            sp.dma_start(wt_raw[:, :, :], w_mem_t).then_inc(ld_wt, 16)
            load_xt(1, 1)
            sp.wait_ge(mt_lo_done, 1)
            load_mt(1)
            sp.dma_start(bias[:, :], b_gate.partition_broadcast(P)).then_inc(ld_bias, 16)
            load_rows(0, 0)
            sp.dma_start(gain[:, :], norm_w.partition_broadcast(P)).then_inc(ld_gain, 16)
            sp.wait_ge(m0_lo_done, 1)
            load_m(1)
            sp.wait_ge(xt_lo_done, GB)
            load_xt(2, 0)
            load_rows(1, 1)
            slots(0, 0, first=True)
            slots(1, 1)
            with sp.Fori(2, NG - 4, 2) as g:
                slots(g, 0)
                slots(g + 1, 1)
            for g in range(NG - 4, NG):
                slots(g, g % 2, left=NG - g)
            store(NG - 1, GB - 2)
            for h, cols in enumerate(HALVES):
                sp.wait_ge(out_done, B + h)
                sp.dma_start(out[NG - 1][:, GB - 1, cols], result[:, GB - 1, cols]).then_inc(stored[GB - 1], 16)
            for b in range(GB - 1):
                sp.wait_ge(stored[b], 16 * NG)
            sp.wait_ge(stored[GB - 1], 16 * (NG + 1))

        @block.gpsimd
        def _(pool):
            pool.memset(power[:, :], -0.5).then_inc(constants, 1)
            pool.memset(eps[:, :], EPS).then_inc(constants, 1)
            pool.memset(ident[:, :], 0.0).then_inc(zeroed, 1)
            pool.wait_ge(zeroed, 1)
            pool.affine_select(out=ident[:, :], in_=ident[:, :], compare_op=ALU.not_equal, fill=1.0,
                               base=0, pattern=[[-1, P]], channel_multiplier=1).then_inc(constants, 1)
            pool.wait_ge(m_hi_done, 1)
            pool.tensor_tensor(m_lo[:, :, :], m_raw[:, :, :], m_hi[:, :, :].bitcast(F32), ALU.subtract).then_inc(m0_lo_done, 1)
            pool.wait_ge(wt_hi_done, 1)
            pool.tensor_tensor(wt_lo[:, :, :], wt_raw[:, :, :], wt_hi[:, :, :].bitcast(F32), ALU.subtract).then_inc(wt_lo_done, 1)
            for b in range(GB):
                pool.wait_ge(xt1_hi_done, b + 1)
                pool.tensor_tensor(xt_lo[:, 1, b], xt_raw[:, 1, b], xt_hi[:, 1, b].bitcast(F32),
                                   ALU.subtract).then_inc(xt1_lo_done, 1)
            pool.wait_ge(constants, 3)
            with pool.Fori(0, NG, 1) as g:
                for b in range(GB):
                    n = GB * g + b
                    pool.wait_ge(sq_done, n + 1)
                    pool.tensor_tensor(safe_sq[:, b:b + 1], mean_sq[:, b:b + 1], eps[:, :],
                                       ALU.add).then_inc(safe_done, 1)
                    pool.wait_ge(safe_done, n + 1)
                    pool.tensor_tensor(inv_rms[:, b:b + 1], safe_sq[:, b:b + 1], power[:, :],
                                       ALU.pow).then_inc(rms_done, 1)

        @block.scalar
        def _(act):
            def hi(dst, src):
                return act.copy(dst, src)

            def split_xt(g, p, b, loads, reuse=True):
                act.wait_ge(ld_xt[p], 16 * loads)
                if reuse:
                    act.wait_ge(gate_made, GB * (g - 2) + b + 1)
                hi(xt_hi[:, p, b], xt_raw[:, p, b]).then_inc(xt_hi_done, 1)

            def split_mt(g, reuse=True):
                act.wait_ge(ld_mt, 16 * (g + 1))
                if reuse:
                    act.wait_ge(s_made, 2 * g)
                hi(mt[:, :, :, 0, :], mt_raw[:, :, :, :]).then_inc(mt_hi_done, 1)

            def split_m(g, reuse=True):
                act.wait_ge(ld_m, 16 * (g + 1))
                if reuse:
                    act.wait_ge(a_made, GB * g)
                hi(m_hi[:, :, :], m_raw[:, :, :]).then_inc(m_hi_done, 1)

            def split_q(g):
                for k in range(EC):
                    act.wait_ge(q_made, EC * g + k + 1)
                    hi(q_hi[:, k], ps_q[k][:, :]).then_inc(q_hi_done, 1)

            def softmax(g):
                for b in range(GB):
                    if b % 2 == 0:
                        act.wait_ge(bias_done, 2 * g + b // 2 + 1)
                    last = act.activation(exps[:, b, :], scores[:, b, :], ACT.Exp,
                                          bias=neg_bias[:, b:b + 1], scale=SCALE,
                                          accum_out=exp_sum[:, b:b + 1])
                last.then_inc(exp_done, 1)

            def split_at(g):
                act.wait_ge(t_made, g + 1)
                hi(at[:, :, 0, :], ps_t[:, :].rearrange("p (b s) -> p b s", b=GB)).then_inc(at_hi_done, 1)

            def split_a(g):
                for b in range(GB):
                    act.wait_ge(a_sum_done, GB * g + b + 1)
                    hi(a_hi[:, b], a_sum[:, b]).then_inc(a_hi_done, 1)

            def square(g, b):
                n = GB * g + b
                act.wait_ge(fused_done, n + 1)
                act.activation(squares[:, b % 2], row[:, b % 2], ACT.Square, scale=SCALE,
                               accum_out=mean_sq[:, b:b + 1]).then_inc(sq_done, 1)

            def tanh(g, b):
                n = GB * g + b
                act.wait_ge(z_done, n + 1)
                act.activation(row[:, b % 2], row[:, b % 2], ACT.Tanh, scale=0.5).then_inc(tanh_done, 1)

            def slots(g, p, loads=None, first=False, last=False, split=True):
                if not (first or last):
                    split_xt(g + 1, 1 - p, GB - 1, loads[0])
                split_a(g)
                if not first:
                    square(g - 1, GB - 1)
                tanh(g, 0)
                if not last:
                    split_mt(g + 1)
                if not last:
                    split_q(g + 1)
                square(g, 0)
                if split:
                    split_xt(g + 2, p, 0, loads[1])
                tanh(g, 1)
                if not last:
                    softmax(g + 1)
                if split:
                    split_xt(g + 2, p, 1, loads[1])
                square(g, 1)
                if not last:
                    split_m(g + 1)
                tanh(g, 2)
                if split:
                    split_xt(g + 2, p, 2, loads[1])
                if not last:
                    split_at(g + 1)
                square(g, 2)
                tanh(g, 3)

            for c in range(DC):
                act.wait_ge(ld_first[c], 32)
                hi(w_hi[:, c, :], w_raw[:, c, :]).then_inc(w_hi_done, 1)
                hi(xt_hi[:, 0, :, c, :], xt_raw[:, 0, :, c, :]).then_inc(xt_hi_done, 1)
            split_mt(0, reuse=False)
            for c in range(DC):
                act.wait_ge(ld_wc[c], 16)
                hi(wc_hi[:, c, :], wc_raw[:, c, :]).then_inc(wc_hi_done, 1)
                if c == 0:
                    split_q(0)
            split_m(0, reuse=False)
            for c in range(DC):
                act.wait_ge(ld_wx[c], 16)
                hi(wx_hi[:, c, :], wx_raw[:, c, :]).then_inc(wx_hi_done, 1)
                if c == 1:
                    softmax(0)
            act.wait_ge(ld_wt, 16)
            hi(wt_hi[:, :, :], wt_raw[:, :, :]).then_inc(wt_hi_done, 1)
            split_at(0)
            for k in range(EC):
                act.wait_ge(wa_made, k + 1)
                hi(wa_hi[:, k, :], ps_ctx[k][:, :]).then_inc(wa_hi_done, 1)
            act.wait_ge(ld_xt[1], 16)
            for b in range(GB):
                hi(xt_hi[:, 1, b], xt_raw[:, 1, b]).then_inc(xt1_hi_done, 1)
            slots(0, 0, loads=(1, 1), first=True)
            slots(1, 1, loads=(1, 2))
            with act.Fori(1, NG // 2 - 1, 1) as h:
                slots(2 * h, 0, loads=(h + 1, h + 1))
                slots(2 * h + 1, 1, loads=(h + 1, h + 2))
            slots(NG - 2, 0, loads=(NG // 2,), split=False)
            slots(NG - 1, 1, split=False, last=True)
            square(NG - 1, GB - 1)

        @block.vector
        def _(dve):
            def lo(dst, src, high):
                return dve.tensor_tensor(dst, src, high.bitcast(F32), ALU.subtract)

            def split_xt(g, p, b):
                dve.wait_ge(xt_hi_done, GB * (g - 1) + b + 1)
                lo(xt_lo[:, p, b], xt_raw[:, p, b], xt_hi[:, p, b]).then_inc(xt_lo_done, 1)

            def split_mt(g):
                dve.wait_ge(mt_hi_done, g + 1)
                lo(mt[:, :, :, 1, :], mt_raw[:, :, :, :], mt[:, :, :, 0, :]).then_inc(mt_lo_done, 1)

            def split_m(g):
                dve.wait_ge(m_hi_done, g + 1)
                lo(m_lo[:, :, :], m_raw[:, :, :], m_hi[:, :, :]).then_inc(m_lo_done, 1)

            def split_q(g):
                for k in range(EC):
                    dve.wait_ge(q_hi_done, EC * g + k + 1)
                    lo(q_lo[:, k], ps_q[k][:, :].rearrange("p (b s) -> p b s", b=GB),
                       q_hi[:, k]).then_inc(q_lo_done, 1)

            def add_halves(dst, bank):
                return dve.tensor_reduce(dst, bank[:, :].rearrange("p (j h s) -> p j s h", j=2, h=2), AX.X, ALU.add)

            def softmax_bias(g):
                for j in range(2):
                    pair = slice(2 * j, 2 * j + 2)
                    n = 2 * g + j + 1
                    dve.wait_ge(s_made, n)
                    add_halves(scores[:, pair, :], ps_s[j]).then_inc(s_sum_done, 1)
                    dve.wait_ge(s_sum_done, n)
                    dve.reduce_max(row_max[:, pair], scores[:, pair, :], AX.X).then_inc(max_done, 1)
                    dve.wait_ge(max_done, n)
                    dve.tensor_scalar(neg_bias[:, pair], row_max[:, pair], -SCALE, None, ALU.mult).then_inc(bias_done, 1)

            def normalise(g):
                dve.wait_ge(exp_done, g + 1)
                dve.reciprocal(inv_sum[:, :], exp_sum[:, :]).then_inc(inv_done, 1)
                dve.wait_ge(inv_done, g + 1)
                dve.tensor_tensor(attn[:, :, :], exps[:, :, :],
                                  inv_sum[:, :].unsqueeze(2).to_broadcast([P, GB, M]), ALU.mult).then_inc(attn_done, 1)

            def split_at(g):
                dve.wait_ge(at_hi_done, g + 1)
                lo(at[:, :, 1, :], ps_t[:, :].rearrange("p (b s) -> p b s", b=GB), at[:, :, 0, :]).then_inc(at_lo_done, 1)

            def sum_a(g, b):
                dve.wait_ge(a_made, GB * g + b + 1)
                add_halves(a_sum[:, b], ps_a[b]).then_inc(a_sum_done, 1)

            def split_a(g, b):
                dve.wait_ge(a_hi_done, GB * g + b + 1)
                lo(a_lo[:, b], a_sum[:, b], a_hi[:, b]).then_inc(a_lo_done, 1)

            def add_bias(g, b, reuse=True):
                if reuse:
                    dve.wait_ge(out_done, GB * g + b - 1)
                dve.wait_ge(gate_made, GB * g + b + 1)
                dve.tensor_tensor(row[:, b % 2], ps_gate[b % 2][:, :], bias[:, :], ALU.add).then_inc(z_done, 1)

            def weigh(g, b):
                n = GB * g + b
                dve.wait_ge(tanh_done, n + 1)
                dve.wait_ge(ctx_made, n + 1)
                dve.scalar_tensor_tensor(out=row[:, b % 2], in0=row[:, b % 2], scalar=1.0, in1=ps_ctx[b % 2][:, :],
                                         op0=ALU.add, op1=ALU.mult).then_inc(u_done, 1)

            def fuse(g, b, p, loads):
                dve.wait_ge(u_done, GB * g + b + 1)
                dve.wait_ge(ld_rows[p], 16 * loads)
                dve.scalar_tensor_tensor(out=row[:, b % 2], in0=row[:, b % 2], scalar=0.5, in1=x_rows[:, p, b, :],
                                         op0=ALU.mult, op1=ALU.add).then_inc(fused_done, 1)

            def finish(g, b, stores=True, cols=slice(0, D)):
                dve.wait_ge(rms_done, GB * g + b + 1)
                if stores:
                    dve.wait_ge(stored[b], 16 * g)
                dve.scalar_tensor_tensor(out=result[:, b, cols], in0=row[:, b % 2, cols], scalar=inv_rms[:, b:b + 1],
                                         in1=gain[:, cols], op0=ALU.mult, op1=ALU.mult).then_inc(out_done, 1)

            def slots(g, p, loads, before=None, first=False, second=False, last=False, split=True):
                for b in range(GB + 1):
                    if b < GB:
                        sum_a(g, b)
                    if b == 0 and not first:
                        fuse(g - 1, GB - 1, 1 - p, before)
                    if b:
                        split_a(g, b - 1)
                    if b == 1 and not (first or last):
                        split_xt(g + 1, 1 - p, GB - 1)
                if first:
                    dve.wait_ge(ld_bias, 16)
                    dve.wait_ge(ld_gain, 16)
                else:
                    finish(g - 1, GB - 2, stores=not second)
                add_bias(g, 0, reuse=not first)
                if not first:
                    finish(g - 1, GB - 1, stores=not second)
                weigh(g, 0)
                fuse(g, 0, p, loads)
                if not last:
                    split_mt(g + 1)
                if not last:
                    split_q(g + 1)
                add_bias(g, 1, reuse=not first)
                if split:
                    split_xt(g + 2, p, 0)
                weigh(g, 1)
                fuse(g, 1, p, loads)
                if not last:
                    softmax_bias(g + 1)
                finish(g, 0, stores=not first)
                if not last:
                    normalise(g + 1)
                if split:
                    split_xt(g + 2, p, 1)
                add_bias(g, 2)
                if not last:
                    split_m(g + 1)
                weigh(g, 2)
                fuse(g, 2, p, loads)
                finish(g, 1, stores=not first)
                if not last:
                    split_at(g + 1)
                add_bias(g, 3)
                if split:
                    split_xt(g + 2, p, 2)
                weigh(g, 3)

            dve.memset(warm[:, :], 0.0).then_inc(warm_ready, 1)
            for c in range(DC):
                dve.wait_ge(w_hi_done, c + 1)
                lo(w_lo[:, c, :], w_raw[:, c, :], w_hi[:, c, :]).then_inc(w_lo_done, 1)
                dve.wait_ge(xt_hi_done, c + 1)
                lo(xt_lo[:, 0, :, c, :], xt_raw[:, 0, :, c, :], xt_hi[:, 0, :, c, :]).then_inc(xt_lo_done, 1)
            split_mt(0)
            for c in range(DC):
                dve.wait_ge(wc_hi_done, c + 1)
                lo(wc_lo[:, c, :], wc_raw[:, c, :], wc_hi[:, c, :]).then_inc(wc_lo_done, 1)
                if c == 0:
                    split_q(0)
            softmax_bias(0)
            for c in range(DC):
                dve.wait_ge(wx_hi_done, c + 1)
                lo(wx_lo[:, c, :], wx_raw[:, c, :], wx_hi[:, c, :]).then_inc(wx_lo_done, 1)
                if c == 1:
                    normalise(0)
            split_at(0)
            for k in range(EC):
                dve.wait_ge(wa_hi_done, k + 1)
                lo(wa_lo[:, k, :], ps_ctx[k][:, :], wa_hi[:, k, :]).then_inc(wa_lo_done, 1)
            slots(0, 0, 1, first=True)
            slots(1, 1, 1, 1, second=True)
            with dve.Fori(1, NG // 2 - 1, 1) as h:
                slots(2 * h, 0, h + 1, h)
                slots(2 * h + 1, 1, h + 1, h + 1)
            slots(NG - 2, 0, NG // 2, NG // 2 - 1, split=False)
            slots(NG - 1, 1, NG // 2, NG // 2, split=False, last=True)
            fuse(NG - 1, GB - 1, 1, NG // 2)
            finish(NG - 1, GB - 2)
            for cols in HALVES:
                finish(NG - 1, GB - 1, cols=cols)

        @block.tensor
        def _(pe):
            def product(dst, left, right, first, end):
                pe.matmul(dst, left[0], right[0], start=first, stop=False)
                pe.matmul(dst, left[0], right[1], start=False, stop=False)
                return pe.matmul(dst, left[1], right[0], start=False, stop=end)

            def side_by_side(dst, left, right, first, end):
                pe.matmul(dst, left[0], right, start=first, stop=False)
                return pe.matmul(dst, left[1], right, start=False, stop=end)

            def chunk(k):
                return slice(k * P, (k + 1) * P)

            def stage_q(g, p, first=False):
                if first:
                    pe.wait_ge(xt1_lo_done, GB)
                else:
                    pe.wait_ge(xt_lo_done, GB * g)
                pe.wait_ge(a_sum_done, GB * g - 2)
                for k in range(EC):
                    for c in range(DC):
                        last = product(ps_q[k][:, :], (w_hi[:, c, chunk(k)], w_lo[:, c, chunk(k)]),
                                       (xt_hi[:, p, :, c, :], xt_lo[:, p, :, c, :]), c == 0, c == DC - 1)
                    last.then_inc(q_made, 1)

            def stage_scores(g, free=True):
                pe.wait_ge(q_lo_done, EC * (g + 1))
                pe.wait_ge(mt_lo_done, g + 1)
                if free:
                    pe.wait_ge(a_sum_done, GB * g)
                for b in range(GB):
                    at_col = b % 2 * 2 * M
                    for k in range(EC):
                        last = side_by_side(ps_s[b // 2][:, at_col:at_col + 2 * M], (q_hi[:, k, b], q_lo[:, k, b]),
                                            mt[:, b, k], k == 0, k == EC - 1)
                    if b % 2:
                        last.then_inc(s_made, 1)

            def stage_transpose(g):
                pe.wait_ge(attn_done, g + 1)
                for b in range(GB):
                    last = pe.transpose(ps_t[:, b * S:(b + 1) * S], attn[:, b, :], ident[:, :])
                last.then_inc(t_made, 1)

            def stage_a(g):
                pe.wait_ge(at_lo_done, g + 1)
                for b in range(GB):
                    for k in range(EC):
                        last = side_by_side(ps_a[b][:, k * 2 * S:(k + 1) * 2 * S],
                                            (m_hi[:, b, chunk(k)], m_lo[:, b, chunk(k)]), at[:, b], True, True)
                    last.then_inc(a_made, 1)

            def gate_x(g, p, b, chunks=range(DC), free=True):
                if free:
                    pe.wait_ge(z_done, GB * g + b - 1)
                for c in chunks:
                    if not free:
                        pe.wait_ge(wx_lo_done, c + 1)
                    product(ps_gate[b % 2][:, :], (xt_hi[:, p, b, c], xt_lo[:, p, b, c]),
                            (wx_hi[:, c], wx_lo[:, c]), c == 0, False)

            def gate_a(g, b):
                pe.wait_ge(a_lo_done, GB * g + b + 1)
                for k in range(EC):
                    last = product(ps_gate[b % 2][:, :], (a_hi[:, b, k], a_lo[:, b, k]),
                                   (wa_hi[:, k], wa_lo[:, k]), False, k == EC - 1)
                last.then_inc(gate_made, 1)

            def context(g, b, free=True):
                if free:
                    pe.wait_ge(u_done, GB * g + b - 1)
                for k in range(EC):
                    last = product(ps_ctx[b % 2][:, :], (a_hi[:, b, k], a_lo[:, b, k]),
                                   (wt_hi[:, k], wt_lo[:, k]), k == 0, k == EC - 1)
                last.then_inc(ctx_made, 1)

            def slots(g, p, first=False, last=False):
                for b in range(GB):
                    if b == 3 and not last:
                        gate_x(g, p, b, range(DC // 2))
                        stage_transpose(g + 1)
                        gate_x(g, p, b, range(DC // 2, DC))
                    elif not (first and b < 2):
                        gate_x(g, p, b)
                    gate_a(g, b)
                    context(g, b, free=not (first and b < 2))
                    if not last:
                        if b == 0:
                            stage_q(g + 1, 1 - p, first=first)
                        elif b == 1:
                            stage_scores(g + 1)
                        elif b == 3:
                            pe.wait_ge(m_lo_done, g + 1)
                            stage_a(g + 1)

            pe.wait_ge(warm_ready, 1)
            for _ in range(WARM_UP):
                pe.matmul(ps_gate[0][:, :], warm[:, 0:P], warm[:, :], start=True, stop=True)
            for c in range(DC):
                pe.wait_ge(w_lo_done, c + 1)
                pe.wait_ge(xt_lo_done, c + 1)
                for k in range(EC):
                    last = product(ps_q[k][:, :], (w_hi[:, c, chunk(k)], w_lo[:, c, chunk(k)]),
                                   (xt_hi[:, 0, :, c, :], xt_lo[:, 0, :, c, :]), c == 0, c == DC - 1)
                    if c == DC - 1:
                        last.then_inc(q_made, 1)
            for c in range(DC):
                pe.wait_ge(wc_lo_done, c + 1)
                for k in range(EC):
                    last = product(ps_ctx[k][:, :], (w_hi[:, c, chunk(k)], w_lo[:, c, chunk(k)]),
                                   (wc_hi[:, c], wc_lo[:, c]), c == 0, c == DC - 1)
                    if c == DC - 1:
                        last.then_inc(wa_made, 1)
                if c == 0:
                    stage_scores(0, free=False)
            pe.wait_ge(constants, 3)
            gate_x(0, 0, 0, range(DC // 2), free=False)
            stage_transpose(0)
            gate_x(0, 0, 0, range(DC // 2, DC), free=False)
            pe.wait_ge(m0_lo_done, 1)
            stage_a(0)
            gate_x(0, 0, 1, free=False)
            pe.wait_ge(wa_lo_done, EC)
            pe.wait_ge(wt_lo_done, 1)
            slots(0, 0, first=True)
            slots(1, 1)
            with pe.Fori(2, NG - 2, 2) as g:
                slots(g, 0)
                slots(g + 1, 1)
            slots(NG - 2, 0)
            slots(NG - 1, 1, last=True)


def kernel(x, ctx_1024, L0_xattn_W_mem, L0_xattn_W_gate, L0_xattn_b_gate, L0_xattn_norm_w):
    import numpy as np
    import concourse.bacc as bacc
    from concourse.bass_utils import run_bass_kernel_spmd

    x, mem = np.asarray(x), np.asarray(ctx_1024)
    w_mem, w_gate = np.asarray(L0_xattn_W_mem), np.asarray(L0_xattn_W_gate)
    laid = {
        "x": x.reshape(NG, GB, S, D).transpose(0, 2, 1, 3),
        "x_t": x.reshape(NG, GB, S, DC, P).transpose(0, 4, 1, 3, 2),
        "mem": mem.reshape(NG, GB, M, E).transpose(0, 2, 1, 3),
        "mem_t": mem.reshape(NG, GB, M, EC, P).transpose(0, 4, 1, 3, 2),
        "w_mem": w_mem.reshape(DC, P, E).transpose(1, 0, 2),
        "w_mem_t": w_mem.reshape(D, EC, P).transpose(2, 1, 0),
        "w_gate_t": w_gate.reshape(D, 2 * DC, P).transpose(2, 1, 0),
        "b_gate": np.asarray(L0_xattn_b_gate),
        "norm_w": np.asarray(L0_xattn_norm_w),
    }
    nc = bacc.Bacc("TRN2", target_bir_lowering=False, num_devices=1)
    arrays = {f"{k}_dram": np.ascontiguousarray(v) for k, v in laid.items()}
    args = [nc.dram_tensor(k, v.shape, mybir.dt.from_np(v.dtype), kind="ExternalInput").ap() for k, v in arrays.items()]
    out = nc.dram_tensor("out_dram", (B, S, D), F32, kind="ExternalOutput").ap()
    gated_cross_attention(nc, *args, out.rearrange("(g b) s d -> g s b d", b=GB))
    r = run_bass_kernel_spmd(nc, [arrays], core_ids=[0])
    return r.results[0]["out_dram"]
```
